# Optimizing a Trainium2 kernel written in Bass

```python
import numpy as np
import jax
import jax.numpy as jnp

def _softmax(x, axis=-1):
    return jax.nn.softmax(x, axis=axis)

def _gelu(x):
    return jax.nn.gelu(x, approximate=True)

def _silu(x):
    return jax.nn.silu(x)

def _sigmoid(x):
    return jax.nn.sigmoid(x)

def _layernorm(x, axis=-1, eps=1e-05):
    m = jnp.mean(x, axis=axis, keepdims=True)
    v = jnp.var(x, axis=axis, keepdims=True)
    return (x - m) / jnp.sqrt(v + eps)

def _scatter_add(tgt, idx, src, axis=0):
    return tgt.at[idx].add(src)

def _segment_sum(src, seg, n):
    return jax.ops.segment_sum(src, seg, n)
kernel_name = 'mk_adaln_ffn_d1_seqx_r2_eb3615'

def setup_inputs(seed: int=0):
    np.random.seed(seed)
    _w = jnp.asarray

    def _rec_inputs():
        import jax
        import jax.numpy as jnp
        _rk = jax.random.key(seed)
        x = -0.0003929 + 0.9999 * jax.random.normal(jax.random.fold_in(_rk, 1), (4, 1024, 512), jnp.float32)
        _lenS = 1024 - jax.random.randint(jax.random.fold_in(_rk, 7), (4,), 0, max(1, 1024 // 4) + 1, jnp.int32)
        _lenS2 = 1024 - jax.random.randint(jax.random.fold_in(_rk, 8), (4,), 0, max(1, 1024 // 4) + 1, jnp.int32)
        itok_B_0_63 = jax.random.randint(jax.random.fold_in(_rk, 11), (4,), 0, 64, jnp.int32)
        return (x, itok_B_0_63)
    x, itok_B_0_63 = _rec_inputs()

    def _L0_cond_setup():
        import jax, jax.numpy as jnp
        import numpy as np
        NUM_CATEGORIES = 64
        INPUT_DIM = 512
        HIDDEN_DIM = 512
        B = 128
        S = 64
        key = jax.random.key(seed)
        kx, kc, kw = jax.random.split(key, 3)
        x = jax.random.normal(kx, (B, S, INPUT_DIM), dtype=jnp.float32)
        cat_ids = jax.random.randint(kc, (B,), 0, NUM_CATEGORIES, dtype=jnp.int32)
        W = 0.02 * jax.random.normal(kw, (NUM_CATEGORIES, INPUT_DIM, HIDDEN_DIM), dtype=jnp.float32)
        b = jnp.zeros((NUM_CATEGORIES, HIDDEN_DIM), dtype=jnp.float32)
        return {'x': x, 'cat_ids': cat_ids, 'W': W, 'b': b}
    _L0_cond_all = _L0_cond_setup()
    _L0_cond_in = {k: v for k, v in _L0_cond_all.items() if k in ('W', 'b')}
    del _L0_cond_all

    def _L0_ffn_setup():
        import math
        import jax, jax.numpy as jnp
        import numpy as np
        B, S, D, F, E = (8, 1024, 512, 2048, 8)
        CAPACITY_FACTOR = 1.0
        key = jax.random.key(seed)
        k1, k2, k3, k4 = jax.random.split(key, 4)
        x = jax.random.normal(k1, (B, S, D), dtype=jnp.float32)
        Wr = jax.random.normal(k2, (D, E), dtype=jnp.float32) * (1.0 / math.sqrt(D))
        W1 = jax.random.normal(k3, (E, D, F), dtype=jnp.float32) * (1.0 / math.sqrt(D))
        W2 = jax.random.normal(k4, (E, F, D), dtype=jnp.float32) * (1.0 / math.sqrt(F))
        return {'x': x, 'Wr': Wr, 'W1': W1, 'W2': W2}
    _L0_ffn_all = _L0_ffn_setup()
    _L0_ffn_in = {k: v for k, v in _L0_ffn_all.items() if k in ('Wr', 'W1', 'W2')}
    del _L0_ffn_all
    return {'x': x, 'itok_B_0_63': itok_B_0_63, 'L0_cond_W': _L0_cond_in['W'], 'L0_cond_b': _L0_cond_in['b'], 'L0_ffn_Wr': _L0_ffn_in['Wr'], 'L0_ffn_W1': _L0_ffn_in['W1'], 'L0_ffn_W2': _L0_ffn_in['W2']}

def reference(x, itok_B_0_63, L0_cond_W, L0_cond_b, L0_ffn_Wr, L0_ffn_W1, L0_ffn_W2):
    import jax
    import jax.numpy as jnp

    def _L0_cond_ref(x, cat_ids, W, b):
        import jax, jax.numpy as jnp
        import numpy as np
        NUM_CATEGORIES = 64
        INPUT_DIM = 512
        HIDDEN_DIM = 512
        B = 128
        S = 64
        selected_W = W[cat_ids]
        selected_b = b[cat_ids]
        out = jnp.einsum('bsd,bdh->bsh', x, selected_W) + selected_b[:, None, :]
        return out

    def _L0_ffn_ref(x, Wr, W1, W2):
        import math
        import jax, jax.numpy as jnp
        import numpy as np
        B, S, D, F, E = (8, 1024, 512, 2048, 8)
        CAPACITY_FACTOR = 1.0
        b, s, d = x.shape
        t = b * s
        cap = max(math.ceil(t * CAPACITY_FACTOR / E), 1)
        xf = x.reshape(t, d)
        probs = jax.nn.softmax(xf.astype(jnp.float32) @ Wr, axis=-1)
        eidx = jnp.argmax(probs, axis=-1)
        p_tok = jnp.take_along_axis(probs, eidx[:, None], axis=1)[:, 0]
        onehot = jax.nn.one_hot(eidx, E, dtype=jnp.int32)
        rank_all = jnp.cumsum(onehot, axis=0) - onehot
        rank = jnp.take_along_axis(rank_all, eidx[:, None], axis=1)[:, 0]
        keep = rank < cap
        slot = jnp.where(keep, rank, cap)
        dispatch = jnp.zeros((E, cap + 1), dtype=jnp.int32).at[eidx, slot].set(jnp.arange(t, dtype=jnp.int32))
        valid = jnp.zeros((E, cap + 1), dtype=bool).at[eidx, slot].set(keep)
        dispatch = dispatch[:, :cap]
        valid = valid[:, :cap]
        xe = xf[dispatch]
        h = jnp.maximum(jnp.einsum('ecd,edf->ecf', xe, W1), 0.0)
        ye = jnp.einsum('ecf,efd->ecd', h, W2)
        pe = p_tok[dispatch]
        ye = ye * (pe * valid.astype(ye.dtype))[:, :, None]
        y = jnp.zeros((t, d), dtype=x.dtype).at[dispatch.reshape(-1)].add(ye.reshape(E * cap, d).astype(x.dtype))
        return y.reshape(b, s, d)
    x = x + _L0_ffn_ref(_L0_cond_ref(x, itok_B_0_63, L0_cond_W, L0_cond_b), L0_ffn_Wr, L0_ffn_W1, L0_ffn_W2)
    return x

_drawn_inputs = setup_inputs


def setup_inputs(seed=0):
    import zlib

    import numpy as np

    out = dict(_drawn_inputs(seed))
    spreads = {'L0_cond_b': (0.0, 0.1)}
    factors = {}
    for name, (base, spread) in spreads.items():
        noise = np.random.default_rng([zlib.crc32(name.encode()), seed]).standard_normal(out[name].shape)
        drawn = base * np.exp(spread * noise) if base else spread * noise
        out[name] = jnp.asarray(drawn.astype(out[name].dtype))
    for name, factor in factors.items():
        out[name] = (out[name] * factor).astype(out[name].dtype)
    return out
```

```python
import concourse.bass as bass
from concourse import mybir
from contextlib import ExitStack



def moe_kernel(nc, x, x_t, cat, cond_w, cond_wt, cond_b, w_r, w_1, w_2, out, h_rows):
    f32, f32r = mybir.dt.float32, mybir.dt.float32r
    bf16, f16, u32 = mybir.dt.bfloat16, mybir.dt.float16, mybir.dt.uint32
    ALU = mybir.AluOpType
    ACTF = mybir.ActivationFunctionType
    AX = mybir.AxisListType

    P = 128
    TOKENS, D = x.shape
    E = w_r.shape[1]
    F = w_1.shape[2]
    CATS = cond_w.shape[0]
    BATCH = cat.shape[1]
    CAP = TOKENS // E
    DK = D // P
    CH = 512
    TPC = CH // P
    NCH = TOKENS // CH
    NT = TOKENS // P
    CPB = NCH // BATCH
    SB = CAP // P
    FT = F // P
    QF = CH // P
    QN = F // CH
    HI, LO = 0, 1

    ROUTE = [3, 5, 7, 9] + [TPC * (c - 1) for c in range(4, NCH)]
    CHOOSE = [n + 1 for n in ROUTE]
    PLACE = [n + 2 for n in ROUTE]
    FILL = [n + 4 for n in ROUTE]
    PRODUCT = [ROUTE[CPB * b] - (2 if b > 1 else 1) for b in range(BATCH)]
    SPLIT_X = [None, (1, 1, 2, 2), (4, 4, 5, 5), (6, 6, 7, 7)] + [range(TPC * (c - 2), TPC * (c - 1)) for c in range(4, NCH)]
    SPLIT_W = [None, (4, 5, 6, 6)] + [tuple(2 * TPC * (b - 1) + n for n in (1, 3, 3, 4)) for b in range(2, BATCH)]
    KEEP_FIRST, KEEP_GATHER, KEEP_BLOCK = 22, 20, 2
    SPLIT_W1 = [NT - 8, NT - 5]
    SPLIT_W2 = [NT - 4, NT - 2]
    Q = 6
    SKIP = 2 * TOKENS

    ctx = ExitStack()
    with ctx:
        def sb(name, shape, dt):
            return ctx.enter_context(nc.sbuf_tensor(name, shape, dt))

        def sem(name):
            return ctx.enter_context(nc.semaphore(name))

        stage = sb("stage", [P, 4, DK, CH], f32)
        w1s = sb("w1_split", [P, 2, 2, DK, CH], f32r)
        w2s = sb("w2_split", [P, 2, 2, DK, CH], f32r)
        xts = sb("xt_split", [P, 4, 2, DK, CH], f32r)
        hts = xts[:, 2, 0, :, :].rearrange("p (r s) c -> p r s c", r=2)
        rows = sb("rows", [P, 2, TPC, D], f32)
        b_rows = sb("b_rows", [P, BATCH, D], f32)
        select = sb("select", [P, 2, TPC, CAP], bf16)
        logits_t = sb("logits_t", [16, 2, CH], f32)
        ident = sb("ident", [P, P], f32)
        iota_c = sb("iota_c", [P, CAP], f16)
        before = sb("before", [P, P], bf16)
        ones = sb("ones", [P, P], bf16)
        wr16 = sb("wr16", [P, DK, 16], f32)
        b_col = sb("b_col", [P, BATCH, DK], f32)
        cat_sb = sb("cat_sb", [1, BATCH], mybir.dt.int32)
        m_split = sb("m_split", [P, DK, 16], f32r)
        bias16 = sb("bias16", [16, 2], f32)
        zeros = sb("zeros", [P, CH], bf16)
        first_e = sb("first_e", [P, TPC, E], f32)
        lg = sb("lg", [P, TPC, E], f32)
        top = sb("top", [P, TPC], f32)
        diff = sb("diff", [P, 2, TPC, E], f32)
        score = sb("score", [P, TPC, E], f32)
        best = sb("best", [P, TPC], f32)
        onehot = sb("onehot", [P, 2, TPC, E], bf16)
        count = sb("count", [P, 2, E], bf16)
        added = sb("added", [P, E], f32)
        expo = sb("expo", [P, 2, TPC, E], f32)
        total = sb("total", [P, TPC], f32)
        prob = sb("prob", [P, TPC], f32)
        rest = sb("rest", [P, TPC], f32)
        payload = sb("payload", [P, NT, Q], bf16)
        packed = sb("packed", [P, 2, TPC, E, Q], bf16)
        ranks = sb("ranks", [P, TPC, E], f32)
        rank = sb("rank", [P, TPC], f32)
        table = sb("table", [P, SB, E, Q], f32)
        tok_f = sb("tok_f", [P, E, SB], f32)
        hole = sb("hole", [P, E, SB], f32)
        tok_all = sb("tok_all", [P, E, SB], u32)
        put_all = sb("put_all", [P, E, SB], u32)
        p_low = sb("p_low", [P, E, SB], f32)
        p_all = sb("p_all", [P, E, SB], f32)
        p_cur = sb("p_cur", [P, SB], f32)

        y_ps = ctx.enter_context(nc.psum_tensor("y_ps", [P, SB, D], f32))
        acc_ps = ctx.enter_context(nc.psum_tensor("acc_ps", [P, 2, CH], f32))
        tp_ps = ctx.enter_context(nc.psum_tensor("tp_ps", [P, 2, CH], f32))
        cond_ps = [acc_ps[:, 0, :], acc_ps[:, 1, :], tp_ps[:, 1, :]]
        table_ps = y_ps[:, 0, 0:SB * E * Q].rearrange("p (s n) -> p s n", s=SB)
        tok_ps = y_ps[:, 1, 0:TPC * 16].rearrange("p (t s) -> p t s", t=TPC)
        rank_ps = y_ps[:, 2, 0:TPC * E]
        m_ps = y_ps[:, 3, 0:DK * E].rearrange("p (m e) -> p m e", m=DK)
        bias_ps = y_ps[0:16, 3, DK * E:DK * E + 1]

        s_cat = sem("cat_loaded")
        s_const = sem("small_loaded")
        s_wr0 = sem("wr_zeroed")
        s_brow = [sem(f"bias_rows{b}_loaded") for b in range(BATCH)]
        s_x0 = [sem(f"first_xt_block{k}") for k in range(DK)]
        s_w0 = [sem(f"first_cond_block{k}") for k in range(DK)]
        s_stage = [sem(f"stage{n}_full") for n in range(4)]
        s_mask = sem("masks_made")
        s_m = sem("m_product_done")
        s_msplit = sem("m_split_done")
        s_xhi = sem("xt_hi_done")
        s_xlo = sem("xt_lo_done")
        s_whi = sem("cond_hi_done")
        s_wlo = sem("cond_lo_done")
        s_lt = sem("logits_t_done")
        s_ltc = sem("logits_t_copied")
        s_lg = sem("logits_done")
        s_diff = sem("diff_done")
        s_exp = sem("exp_done")
        s_oh = sem("onehot_done")
        s_rank = sem("rank_done")
        s_sel = sem("select_done")
        s_tab = sem("table_step_done")
        s_dve = sem("vector_chain")
        s_acc = sem("acc_full")
        s_accf = sem("acc_free")
        s_hlast = sem("last_h_stored")
        s_hst = [sem(f"h_stored{n}") for n in range(2)]
        s_keep = sem("x_copied")
        s_idx = sem("tables_ready")
        s_hhi = sem("hidden_hi_done")
        s_w1hi = sem("w1_hi_done")
        s_w1lo = sem("w1_lo_done")
        s_w2hi = sem("w2_hi_done")
        s_w2lo = sem("w2_lo_done")
        s_tp = sem("xe_transposed")
        s_xehi = sem("xe_hi_done")
        s_xelo = sem("xe_lo_done")
        s_f2 = sem("outputs_full")
        s_pcur = sem("p_cur_done")
        s_y = sem("y_ps_read")
        s_hg = [sem(f"h_gathered{n}") for n in range(SB)]
        s_rows = sem("h_rows_here")
        s_xg = sem("x_gathered")
        s_put = sem("scattered")

        A_LOADS = [BATCH, BATCH - 1, BATCH - 1, BATCH]

        w1_v = w_1.rearrange("e (k p) f -> p e k f", p=P)
        w2_v = w_2.rearrange("e (q k p) d -> p (e q) k d", p=P, k=DK)
        xt_v = x_t.rearrange("(k p) n -> p k n", p=P)
        h_v = h_rows.rearrange("(c t p) d -> p c t d", p=P, t=TPC)

        block = ctx.enter_context(nc.Block())

        @block.sync
        def _(sp):
            def load_w1(e, q, slot):
                sp.dma_start(stage[:, slot, :, :],
                             w1_v[:, bass.ds(e, 1), :, q * CH:(q + 1) * CH].rearrange("p o k f -> p (o k) f")
                             ).then_inc(s_stage[slot], 16)

            def load_w2(n, slot):
                sp.dma_start(stage[:, 2 + slot, :, :],
                             w2_v[:, bass.ds(n, 1), :, :].rearrange("p o k d -> p (o k) d")
                             ).then_inc(s_stage[2 + slot], 16)

            sp.dma_start(cat_sb[0:1, :], cat).then_inc(s_cat, 16)
            sp.wait_ge(s_cat, 16)
            cats = [sp.value_load(cat_sb[0:1, b:b + 1], min_val=0, max_val=CATS - 1) for b in range(BATCH)]

            def cond_view(b):
                return cond_w[bass.ds(cats[b], 1), :, :].rearrange("o (k p) h -> p (o k) h", p=P)

            for k in range(DK):
                sp.dma_start(stage[:, 1, k, :], cond_view(0)[:, k, :]).then_inc(s_w0[k], 16)
            def load_cond_wt(b):
                sp.dma_start(stage[:, 0, :, :], cond_wt[bass.ds(cats[b], 1), :, :].rearrange(
                    "o (p k) d -> p (o k) d", p=P)).then_inc(s_stage[0], 16)

            def load_xt(c):
                sp.dma_start(stage[:, 2 + c % 2, :, :], xt_v[:, :, c * CH:(c + 1) * CH]
                             ).then_inc(s_stage[2 + c % 2], 16)

            def copy_x(b):
                n = TOKENS // BATCH
                sp.dma_start(out[b * n:(b + 1) * n, :], x[b * n:(b + 1) * n, :]).then_inc(s_keep, 16)

            load_xt(1)

            def load_bias_rows(b):
                sp.dma_start(b_rows[:, b, :], cond_b[bass.ds(cats[b], 1), :].to_broadcast([P, D])
                             ).then_inc(s_brow[b], 16)

            load_bias_rows(0)
            load_cond_wt(0)
            sp.wait_ge(s_wr0, 1)
            sp.dma_start(wr16[:, :, 0:E], w_r.rearrange("(p k) e -> p k e", p=P)).then_inc(s_const, 16)
            for b in range(BATCH):
                sp.dma_start(b_col[:, b, :], cond_b[bass.ds(cats[b], 1), :].rearrange("o (p k) -> p (o k)", p=P)
                             ).then_inc(s_const, 16)
            for b in range(1, BATCH):
                sp.wait_ge(s_xlo, DK * (CPB * b - 1))
                load_xt(CPB * b)
                sp.wait_ge(s_wlo, DK * b)
                sp.dma_start(stage[:, 1, :, :], cond_view(b)).then_inc(s_stage[1], 16)
                sp.wait_ge(s_m, b)
                load_cond_wt(b)
                sp.wait_ge(s_xlo, DK * CPB * b)
                load_xt(CPB * b + 1)
                load_bias_rows(b)
                copy_x(b)
            sp.wait_ge(s_m, BATCH)
            load_w1(0, 0, 0)
            sp.wait_ge(s_xlo, DK * (NCH - 1))
            load_w2(0, 0)
            sp.wait_ge(s_wlo, DK * BATCH)
            load_w1(0, 1, 1)
            sp.wait_ge(s_xlo, DK * NCH)
            load_w2(1, 1)
            copy_x(0)

            for t in range(TPC):
                sp.wait_ge(s_accf, TPC * (NCH - 1) + t + 1)
                sp.dma_start(h_v[:, NCH - 1, t, :], rows[:, (NCH - 1) % 2, t, :]).then_inc(s_hlast, 16)

            def load_later(e, q):
                later = q + 2
                sp.wait_ge(s_w1lo, e * (2 * QN) + 2 * (q + 1))
                load_w1(e + later // QN, later % QN, q % 2)
                sp.wait_ge(s_w2lo, e * (2 * QN) + 2 * (q + 1))
                load_w2(e * QN + later, q % 2)

            for s in range(SB):
                sp.wait_ge(s_hg[s], 16)
            with sp.Fori(0, E - 1) as e:
                for q in range(QN):
                    load_later(e, q)
            for q in range(QN - 2):
                load_later(E - 1, q)
            sp.wait_ge(s_w1lo, 2 * (E * QN - 1))
            sp.sem_inc(s_stage[0], 16)
            sp.wait_ge(s_w2lo, 2 * (E * QN - 1))
            sp.sem_inc(s_stage[2], 16)

        @block.gpsimd
        def _(pool):
            nc.gpsimd.memset(ones[:, :], 1.0).then_inc(s_mask, 1)
            nc.gpsimd.memset(zeros[:, :], 0.0).then_inc(s_mask, 1)
            nc.gpsimd.memset(wr16[:, :, :], 0.0).then_inc(s_wr0, 1)
            nc.gpsimd.memset(ident[:, :], 0.0).then_inc(s_mask, 1)
            nc.gpsimd.memset(before[:, :], 1.0).then_inc(s_mask, 1)
            nc.gpsimd.memset(payload[:, :, :], 1.0).then_inc(s_mask, 1)
            nc.gpsimd.memset(count[:, 0, :], 0.0).then_inc(s_mask, 1)
            pool.wait_ge(s_mask, 6)
            nc.gpsimd.affine_select(out=ident[:, :], in_=ident[:, :], compare_op=ALU.not_equal, fill=1.0,
                                    base=0, pattern=[[-1, P]], channel_multiplier=1).then_inc(s_mask, 1)
            nc.gpsimd.affine_select(out=before[:, :], in_=before[:, :], compare_op=ALU.is_gt, fill=0.0,
                                    base=0, pattern=[[1, P]], channel_multiplier=-1).then_inc(s_mask, 1)
            nc.gpsimd.iota(iota_c[:, :], pattern=[[1, CAP]], base=0, channel_multiplier=0,
                           allow_small_or_imprecise_dtypes=True).then_inc(s_mask, 1)
            nc.gpsimd.iota(first_e[:, :, :], pattern=[[0, TPC], [-1, E]], base=E, channel_multiplier=0,
                           allow_small_or_imprecise_dtypes=True).then_inc(s_mask, 1)
            nc.gpsimd.iota(payload[:, :, 0], pattern=[[1, NT]], base=0, channel_multiplier=0,
                           allow_small_or_imprecise_dtypes=True).then_inc(s_mask, 1)
            nc.gpsimd.iota(payload[:, :, 1], pattern=[[0, NT]], base=0, channel_multiplier=1,
                           allow_small_or_imprecise_dtypes=True).then_inc(s_mask, 1)

            for c in range(NCH - 1):
                pool.wait_ge(s_accf, TPC * (c + 1))
                pool.dma_start(h_v[:, c, :, :], rows[:, c % 2, :, :]).then_inc(s_hst[c % 2], 16)

            def gather(which, source, e, done):
                for s in range(SB):
                    pool.indirect_dma_start(
                        out=rows[:, which, s, :], out_offset=None, in_=source,
                        in_offset=bass.IndirectOffsetOnAxis(ap=tok_all[:, e, s:s + 1], axis=0),
                        bounds_check=TOKENS - 1, oob_is_err=False).then_inc(done[s], 16)

            pool.wait_ge(s_idx, 1)
            pool.wait_ge(s_hst[0], 16 * (NCH // 2))
            pool.wait_ge(s_hst[1], 16 * (NCH // 2 - 1))
            pool.wait_ge(s_hlast, 16 * TPC)
            gather(0, h_rows, 0, s_hg)
            gather(1, x, 0, [s_xg] * SB)
            pool.wait_ge(s_tp, DK)
            gather(0, h_rows, 1, s_hg)
            pool.wait_ge(s_keep, 16 * BATCH)
            for e in range(E):
                for s in range(SB):
                    pool.wait_ge(s_hg[s], 16 * min(e + 2, E))
                pool.sem_inc(s_rows, 1)
                if e + 2 < E:
                    pool.wait_ge(s_tp, DK * (e + 2))
                    gather(0, h_rows, e + 2, s_hg)
                for s in range(SB):
                    pool.wait_ge(s_y, SB * e + s + 2)
                    pool.indirect_dma_start(
                        out=out, out_offset=bass.IndirectOffsetOnAxis(ap=put_all[:, e, s:s + 1], axis=0),
                        in_=rows[:, 1, s, :], in_offset=None,
                        bounds_check=TOKENS - 1, oob_is_err=False).then_inc(s_put, 16)
                pool.wait_ge(s_put, 16 * SB * (e + 1))
                if e + 1 < E:
                    gather(1, x, e + 1, [s_xg] * SB)

        @block.scalar
        def _(act):
            def split_xt(c, k):
                if c == 0:
                    act.wait_ge(s_x0[k], 16)
                else:
                    slot = 2 + c % 2
                    act.wait_ge(s_stage[slot], 16 * ((c + 1) // 2))
                if c >= 4:
                    act.wait_ge(s_acc, TPC * (c - 3))
                nc.scalar.activation(xts[:, c % 4, HI, k, :], stage[:, 2 + c % 2, k, :], ACTF.Copy
                                     ).then_inc(s_xhi, 1)

            def split_cond(b, k):
                if b == 0:
                    act.wait_ge(s_w0[k], 16)
                else:
                    act.wait_ge(s_stage[1], 16 * b)
                if b >= 2:
                    act.wait_ge(s_acc, TPC * CPB * (b - 1))
                nc.scalar.activation(w2s[:, b % 2, HI, k, :], stage[:, 1, k, :], ACTF.Copy
                                     ).then_inc(s_whi, 1)

            def copy_logits(c):
                act.wait_ge(s_msplit, c // CPB + 1)
                act.wait_ge(s_lt, c + 1)
                if c >= 2:
                    act.wait_ge(s_lg, c - 1)
                nc.scalar.activation(logits_t[:, c % 2, :], tp_ps[0:16, 0, :], ACTF.Identity,
                                     bias=bias16[:, (c // CPB) % 2:(c // CPB) % 2 + 1]).then_inc(s_ltc, 1)

            def exps(c):
                act.wait_ge(s_diff, c + 1)
                nc.scalar.activation(expo[:, c % 2, :, :], diff[:, c % 2, :, :], ACTF.Exp).then_inc(s_exp, 1)

            def split_w1(half, stage_count, slot):
                act.wait_ge(s_stage[slot], stage_count)
                ks = slice(2 * half, 2 * half + 2)
                nc.scalar.activation(w1s[:, slot, HI, ks, :], stage[:, slot, ks, :], ACTF.Copy
                                     ).then_inc(s_w1hi, 1)

            def split_w2(half, stage_count, slot):
                act.wait_ge(s_stage[2 + slot], stage_count)
                ks = slice(2 * half, 2 * half + 2)
                nc.scalar.activation(w2s[:, slot, HI, ks, :], stage[:, 2 + slot, ks, :], ACTF.Copy
                                     ).then_inc(s_w2hi, 1)

            for k in range(DK):
                act.dma_start(stage[:, 2, k, :], xt_v[:, k, 0:CH]).then_inc(s_x0[k], 16)
            for k in range(DK):
                split_xt(0, k)
            for k in range(DK):
                split_cond(0, k)
            for n in range(NT):
                for c in range(1, NCH):
                    for k in range(DK):
                        if SPLIT_X[c][k] == n:
                            split_xt(c, k)
                for b in range(1, BATCH):
                    for k in range(DK):
                        if SPLIT_W[b][k] == n:
                            split_cond(b, k)
                if n in ROUTE:
                    copy_logits(ROUTE.index(n))
                if n in CHOOSE:
                    exps(CHOOSE.index(n))
                if n in SPLIT_W1:
                    split_w1(SPLIT_W1.index(n), 16 * (A_LOADS[0] + 1), 0)
                if n in SPLIT_W2:
                    split_w2(SPLIT_W2.index(n), 16 * (A_LOADS[2] + 1), 0)

            def split_xe(n, par, k, bank):
                act.wait_ge(s_tp, n + 1)
                nc.scalar.activation(xts[:, par, HI, k, :], bank, ACTF.Copy).then_inc(s_xehi, 1)

            for k in range(DK):
                split_xe(k, 0, k, y_ps[:, k, :])

            with act.Fori(0, E // 2) as pair:
                for par in range(2):
                    for j in range(FT):
                        q, m = j // QF, j % QF
                        tile = pair * (2 * FT) + par * FT + j
                        act.wait_ge(s_acc, NT + 1 + tile)
                        nc.scalar.activation(hts[:, j % 2, HI, :], acc_ps[:, j % 2, :], ACTF.Relu
                                             ).then_inc(s_hhi, 1)
                        slot = (q + 1) % 2
                        full = pair * (16 * QN) + 16 * ((par * QN + q + 1) // 2 + 1)
                        if m < 2:
                            split_w1(m, full + 16 * A_LOADS[slot], slot)
                        else:
                            split_w2(m - 2, full + 16 * A_LOADS[2 + slot], slot)
                        if FT // 2 - 2 <= j < FT // 2 - 2 + DK:
                            k = j - (FT // 2 - 2)
                            split_xe(pair * (2 * DK) + (par + 1) * DK + k, 1 - par, k, tp_ps[:, k % 2, :])

        @block.vector
        def _(dve):
            chained = [0]

            def then(ins):
                chained[0] += 1
                ins.then_inc(s_dve, 1)
                dve.wait_ge(s_dve, chained[0])

            def split_xt(c, k):
                dve.wait_ge(s_xhi, DK * c + k + 1)
                nc.vector.tensor_tensor(xts[:, c % 4, LO, k, :], stage[:, 2 + c % 2, k, :],
                                        xts[:, c % 4, HI, k, :].bitcast(f32), ALU.subtract).then_inc(s_xlo, 1)

            def split_cond(b, k):
                dve.wait_ge(s_whi, DK * b + k + 1)
                nc.vector.tensor_tensor(w2s[:, b % 2, LO, k, :], stage[:, 1, k, :],
                                        w2s[:, b % 2, HI, k, :].bitcast(f32), ALU.subtract).then_inc(s_wlo, 1)

            def split_m(b):
                dve.wait_ge(s_m, b + 1)
                then(nc.vector.tensor_copy(m_split[:, :, 0:E], m_ps))
                nc.vector.tensor_tensor(m_split[:, :, E:2 * E], m_ps, m_split[:, :, 0:E].bitcast(f32),
                                        ALU.subtract)
                if b >= 2:
                    dve.wait_ge(s_ltc, CPB * (b - 1))
                nc.vector.tensor_copy(bias16[:, b % 2:b % 2 + 1], bias_ps).then_inc(s_msplit, 1)

            def store_h(c, t):
                n = TPC * c + t
                if t == 0 and c >= 2:
                    dve.wait_ge(s_hst[c % 2], 16 * (c // 2))
                dve.wait_ge(s_acc, n + 1)
                if n % (TPC * CPB) == 0:
                    dve.wait_ge(s_brow[c // CPB], 16)
                nc.vector.tensor_tensor(rows[:, c % 2, t, :], cond_ps[n % 3], b_rows[:, c // CPB, :],
                                        ALU.add).then_inc(s_accf, 1)

            def wide(v):
                return v.unsqueeze(2).to_broadcast([P, TPC, E])

            def choose(c):
                par = c % 2
                dve.wait_ge(s_lg, c + 1)
                then(nc.vector.tensor_reduce(lg[:, :, :], tok_ps.rearrange("p t (s e) -> p t e s", s=2),
                                             AX.X, ALU.add))
                then(nc.vector.tensor_reduce(top[:, :], lg[:, :, :], AX.X, ALU.max))
                if c >= 2:
                    dve.wait_ge(s_exp, c - 1)
                chained[0] += 1
                nc.vector.tensor_tensor(diff[:, par, :, :], lg[:, :, :], wide(top[:, :]), ALU.subtract
                                        ).then_inc(s_diff, 1)
                chained[0] -= 1
                dve.wait_ge(s_diff, c + 1)
                then(nc.vector.scalar_tensor_tensor(score[:, :, :], diff[:, par, :, :], 0.0, first_e[:, :, :],
                                                    ALU.is_equal, ALU.mult))
                then(nc.vector.tensor_reduce(best[:, :], score[:, :, :], AX.X, ALU.max))
                then(nc.vector.tensor_tensor(onehot[:, par, :, :], score[:, :, :], wide(best[:, :]), ALU.is_equal))
                then(nc.vector.tensor_reduce(added[:, :], onehot[:, par, :, :].rearrange("p t e -> p e t"),
                                             AX.X, ALU.add))
                nc.vector.tensor_tensor(count[:, 1 - par, :], count[:, par, :], added[:, :], ALU.add
                                        ).then_inc(s_oh, 1)

            def place(c):
                par = c % 2
                tiles = slice(TPC * c, TPC * (c + 1))
                dve.wait_ge(s_exp, c + 1)
                then(nc.vector.tensor_reduce(total[:, :], expo[:, par, :, :], AX.X, ALU.add))
                then(nc.vector.reciprocal(prob[:, :], total[:, :]))
                then(nc.vector.tensor_copy(payload[:, tiles, 3], prob[:, :]))
                then(nc.vector.tensor_tensor(rest[:, :], prob[:, :], payload[:, tiles, 3], ALU.subtract))
                then(nc.vector.tensor_copy(payload[:, tiles, 4], rest[:, :]))
                then(nc.vector.tensor_tensor(payload[:, tiles, 5], rest[:, :], payload[:, tiles, 4], ALU.subtract))
                if c >= 2:
                    dve.wait_ge(s_tab, c - 1)
                nc.vector.tensor_tensor(packed[:, par, :, :, :],
                                        onehot[:, par, :, :].unsqueeze(3).to_broadcast([P, TPC, E, Q]),
                                        payload[:, tiles, :].unsqueeze(2).to_broadcast([P, TPC, E, Q]),
                                        ALU.mult)
                dve.wait_ge(s_rank, c + 1)
                then(nc.vector.tensor_tensor(ranks[:, :, :], rank_ps.rearrange("p (t e) -> p t e", t=TPC),
                                             onehot[:, par, :, :], ALU.mult))
                then(nc.vector.tensor_reduce(rank[:, :], ranks[:, :, :], AX.X, ALU.add))
                for t in range(TPC):
                    last = nc.vector.tensor_scalar(select[:, par, t, :], iota_c[:, :], rank[:, t:t + 1], None,
                                                   ALU.is_equal)
                last.then_inc(s_sel, 1)

            def split_w1(half, count, slot):
                dve.wait_ge(s_w1hi, count)
                ks = slice(2 * half, 2 * half + 2)
                nc.vector.tensor_tensor(w1s[:, slot, LO, ks, :], stage[:, slot, ks, :],
                                        w1s[:, slot, HI, ks, :].bitcast(f32), ALU.subtract).then_inc(s_w1lo, 1)

            def split_w2(half, count, slot):
                dve.wait_ge(s_w2hi, count)
                ks = slice(2 * half, 2 * half + 2)
                nc.vector.tensor_tensor(w2s[:, slot, LO, ks, :], stage[:, 2 + slot, ks, :],
                                        w2s[:, slot, HI, ks, :].bitcast(f32), ALU.subtract).then_inc(s_w2lo, 1)

            def make_tables():
                by_e = "p s e -> p e s"
                dve.wait_ge(s_tab, NCH)
                then(nc.vector.tensor_copy(table[:, :, :, :].rearrange("p s e q -> p s (e q)"),
                                           table_ps))
                then(nc.vector.scalar_tensor_tensor(tok_f[:, :, :], table[:, :, :, 0].rearrange(by_e), float(P),
                                                    table[:, :, :, 1].rearrange(by_e), ALU.mult, ALU.add))
                then(nc.vector.tensor_copy(tok_all[:, :, :], tok_f[:, :, :]))
                then(nc.vector.tensor_scalar(hole[:, :, :], table[:, :, :, 2].rearrange(by_e), -float(SKIP),
                                             float(SKIP), ALU.mult, ALU.add))
                then(nc.vector.tensor_tensor(put_all[:, :, :], tok_f[:, :, :], hole[:, :, :], ALU.add))
                then(nc.vector.tensor_tensor(p_low[:, :, :], table[:, :, :, 4].rearrange(by_e),
                                             table[:, :, :, 5].rearrange(by_e), ALU.add))
                nc.vector.tensor_tensor(p_all[:, :, :], table[:, :, :, 3].rearrange(by_e), p_low[:, :, :],
                                        ALU.add).then_inc(s_idx, 1)

            for k in range(DK):
                split_xt(0, k)
            for k in range(DK):
                split_cond(0, k)
            for n in range(NT):
                store_h(n // TPC, n % TPC)
                if n == 0:
                    dve.wait_ge(s_mask, 12)
                for c in range(1, NCH):
                    for k in range(DK):
                        if SPLIT_X[c][k] == n:
                            split_xt(c, k)
                for b in range(1, BATCH):
                    for k in range(DK):
                        if SPLIT_W[b][k] == n:
                            split_cond(b, k)
                if n in CHOOSE:
                    choose(CHOOSE.index(n))
                if n in PLACE:
                    place(PLACE.index(n))
                if n in PRODUCT:
                    split_m(PRODUCT.index(n))
                if n in SPLIT_W1:
                    split_w1(SPLIT_W1.index(n), SPLIT_W1.index(n) + 1, 0)
                if n in SPLIT_W2:
                    split_w2(SPLIT_W2.index(n), SPLIT_W2.index(n) + 1, 0)
                if n == FILL[-1] + 1:
                    make_tables()

            def split_xe(n, par, k, bank):
                dve.wait_ge(s_xehi, n + 1)
                nc.vector.tensor_tensor(xts[:, par, LO, k, :], bank,
                                        xts[:, par, HI, k, :].bitcast(f32), ALU.subtract).then_inc(s_xelo, 1)

            for k in range(DK):
                split_xe(k, 0, k, y_ps[:, k, :])
            dve.wait_ge(s_idx, 1)
            dve.sem_inc(s_y, 1)

            with dve.Fori(0, E // 2) as pair:
                for par in range(2):
                    e = pair * 2 + par
                    for j in range(FT):
                        q, m = j // QF, j % QF
                        tile = pair * (2 * FT) + par * FT + j
                        dve.wait_ge(s_hhi, tile + 1)
                        nc.vector.scalar_tensor_tensor(hts[:, j % 2, LO, :], acc_ps[:, j % 2, :], 0.0,
                                                       hts[:, j % 2, HI, :].bitcast(f32), ALU.max, ALU.subtract
                                                       ).then_inc(s_accf, 1)
                        slot = (q + 1) % 2
                        halves = pair * (4 * QN) + 2 * (par * QN + q + 1)
                        if m < 2:
                            split_w1(m, halves + m + 1, slot)
                        else:
                            split_w2(m - 2, halves + m - 1, slot)
                        if FT // 2 - 2 <= j < FT // 2 - 2 + DK:
                            k = j - (FT // 2 - 2)
                            split_xe(pair * (2 * DK) + (par + 1) * DK + k, 1 - par, k, tp_ps[:, k % 2, :])
                    dve.wait_ge(s_y, e * SB + 1)
                    nc.vector.tensor_copy(p_cur[:, :], p_all[:, bass.ds(e, 1), :].rearrange("p o s -> p (o s)")
                                          ).then_inc(s_pcur, 1)
                    dve.wait_ge(s_pcur, e + 1)
                    dve.wait_ge(s_xg, e * 64 + 64)
                    for s in range(SB):
                        dve.wait_ge(s_f2, e * SB + s + 1)
                        nc.vector.scalar_tensor_tensor(rows[:, 1, s, :], y_ps[:, s, :], p_cur[:, s:s + 1],
                                                       rows[:, 1, s, :], ALU.mult, ALU.add).then_inc(s_y, 1)

        @block.tensor
        def _(pe):
            PARTS = ((HI, HI), (HI, LO), (LO, HI))

            def m_product(b):
                pe.wait_ge(s_stage[0], 16 * (b + 1))
                if b == 0:
                    pe.wait_ge(s_const, 16 * (BATCH + 1))
                else:
                    pe.wait_ge(s_msplit, b)
                for m in range(DK):
                    for k in range(DK):
                        nc.tensor.matmul(m_ps[:, m, :], stage[:, 0, k, m * P:(m + 1) * P], wr16[:, k, 0:E],
                                         start=(k == 0), stop=(k == DK - 1))
                for k in range(DK):
                    last = nc.tensor.matmul(bias_ps, wr16[:, k, :], b_col[:, b, k:k + 1],
                                            start=(k == 0), stop=(k == DK - 1))
                last.then_inc(s_m, 1)

            def route(c):
                pe.wait_ge(s_msplit, c // CPB + 1)
                pe.wait_ge(s_xlo, DK * (c + 1))
                if c >= 1:
                    pe.wait_ge(s_ltc, c)
                for k in range(DK):
                    for part in (HI, LO):
                        last = nc.tensor.matmul(tp_ps[0:16, 0, :], m_split[:, k, :], xts[:, c % 4, part, k, :],
                                                start=(k == 0 and part == HI), stop=(k == DK - 1 and part == LO))
                last.then_inc(s_lt, 1)

            def by_token(c):
                pe.wait_ge(s_ltc, c + 1)
                if c >= 1:
                    pe.wait_ge(s_oh, c)
                for t in range(TPC):
                    last = nc.tensor.transpose(tok_ps[:, t, :], logits_t[:, c % 2, t * P:(t + 1) * P],
                                               ident[0:16, 0:16])
                last.then_inc(s_lg, 1)

            def rank_of(c):
                pe.wait_ge(s_oh, c + 1)
                if c >= 1:
                    pe.wait_ge(s_sel, c)
                nc.tensor.matmul(rank_ps, before[:, :], onehot[:, c % 2, :, :].rearrange("p t e -> p (t e)"),
                                 start=True, stop=False)
                for t in range(TPC - 1):
                    later = TPC - 1 - t
                    nc.tensor.matmul(rank_ps[:, (t + 1) * E:], ones[:, :],
                                     onehot[:, c % 2, t:t + 1, :].to_broadcast([P, later, E]),
                                     start=False, stop=False)
                nc.tensor.matmul(rank_ps, ones[:, :],
                                 count[:, c % 2, :].unsqueeze(1).to_broadcast([P, TPC, E]),
                                 start=False, stop=True).then_inc(s_rank, 1)

            def fill_table(c):
                pe.wait_ge(s_sel, c + 1)
                for t in range(TPC):
                    for s in range(SB):
                        last = nc.tensor.matmul(table_ps[:, s, :], select[:, c % 2, t, s * P:(s + 1) * P],
                                                packed[:, c % 2, t, :, :].rearrange("p e q -> p (e q)"),
                                                start=False, stop=(c, t, s) == (NCH - 1, TPC - 1, SB - 1))
                last.then_inc(s_tab, 1)

            def open_table():
                nc.tensor.matmul(table_ps.rearrange("p s n -> p (s n)"), ones[:, :], zeros[:, 0:SB * E * Q],
                                 start=True, stop=False)

            def cond_tile(c, t):
                n = TPC * c + t
                if t == 0 and n > 0:
                    pe.wait_ge(s_xlo, DK * (c + 1))
                    pe.wait_ge(s_wlo, DK * (c // CPB + 1))
                if n >= 3:
                    pe.wait_ge(s_accf, n - 2)
                for k in range(DK):
                    if n == 0:
                        pe.wait_ge(s_wlo, k + 1)
                    for a, w in PARTS:
                        last = nc.tensor.matmul(cond_ps[n % 3], xts[:, c % 4, a, k, t * P:(t + 1) * P],
                                                w2s[:, (c // CPB) % 2, w, k, :],
                                                start=(k == 0 and (a, w) == (HI, HI)),
                                                stop=(k == DK - 1 and (a, w) == (LO, HI)))
                last.then_inc(s_acc, 1)

            def keep_warm(times):
                for _ in range(times):
                    nc.tensor.matmul(acc_ps[:, 1, :], ones[:, :], zeros[:, :], start=True, stop=True)

            pe.wait_ge(s_mask, 2)
            keep_warm(KEEP_FIRST)
            for n in range(NT):
                cond_tile(n // TPC, n % TPC)
                if n == 0:
                    pe.wait_ge(s_mask, 12)
                    open_table()
                if n in FILL:
                    fill_table(FILL.index(n))
                if n in PRODUCT:
                    m_product(PRODUCT.index(n))
                if n in ROUTE:
                    route(ROUTE.index(n))
                if n in CHOOSE:
                    by_token(CHOOSE.index(n))
                if n in PLACE:
                    rank_of(PLACE.index(n))

            def transpose_block(bank, s, k):
                return nc.tensor.transpose(bank[:, s * P:(s + 1) * P], rows[:, 0, s, k * P:(k + 1) * P], ident[:, :])

            pe.wait_ge(s_accf, NT)
            keep_warm(KEEP_GATHER)
            for s in range(SB):
                pe.wait_ge(s_hg[s], 16)
                for k in range(DK):
                    last = transpose_block(y_ps[:, k, :], s, k)
                    if s == SB - 1:
                        last.then_inc(s_tp, 1)
                if s < SB - 1:
                    keep_warm(KEEP_BLOCK)

            with pe.Fori(0, E // 2) as pair:
                for par in range(2):
                    def second(j):
                        slot, kk = (j // QF) % 2, j % QF
                        tile = pair * (2 * FT) + par * FT + j
                        if kk == 0:
                            pe.wait_ge(s_w2lo, pair * (4 * QN) + 2 * (par * QN + j // QF + 1))
                        if j == 0:
                            pe.wait_ge(s_y, pair * (2 * SB) + par * SB + 1)
                        pe.wait_ge(s_accf, NT + 1 + tile)
                        for s in range(SB):
                            for a, w in PARTS:
                                last = nc.tensor.matmul(y_ps[:, s, :], hts[:, j % 2, a, s * P:(s + 1) * P],
                                                        w2s[:, slot, w, kk, :],
                                                        start=(j == 0 and (a, w) == (HI, HI)),
                                                        stop=(j == FT - 1 and (a, w) == (LO, HI)))
                            if j == FT - 1:
                                last.then_inc(s_f2, 1)

                    for j in range(FT):
                        slot, jj = (j // QF) % 2, j % QF
                        tile = pair * (2 * FT) + par * FT + j
                        if jj == 0:
                            pe.wait_ge(s_w1lo, pair * (4 * QN) + 2 * (par * QN + j // QF + 1))
                        pe.wait_ge(s_accf, NT - 1 + tile)
                        for k in range(DK):
                            if j == 0:
                                pe.wait_ge(s_xelo, pair * (2 * DK) + par * DK + k + 1)
                            for w, a in PARTS:
                                last = nc.tensor.matmul(acc_ps[:, j % 2, :], w1s[:, slot, w, k, jj * P:(jj + 1) * P],
                                                        xts[:, par, a, k, :],
                                                        start=(k == 0 and (w, a) == (HI, HI)),
                                                        stop=(k == DK - 1 and (w, a) == (LO, HI)))
                        last.then_inc(s_acc, 1)
                        if FT // 2 - 2 <= j < FT // 2 - 2 + DK:
                            k = j - (FT // 2 - 2)
                            if k == 0:
                                pe.wait_ge(s_rows, pair * 2 + par + 1)
                            pe.wait_ge(s_xelo, pair * (2 * DK) + (par + 1) * DK + k - 1)
                            for s in range(SB):
                                last = transpose_block(tp_ps[:, k % 2, :], s, k)
                            last.then_inc(s_tp, 1)
                        if j >= 1:
                            second(j - 1)
                    second(FT - 1)


def kernel(**inputs):
    import numpy as np
    import concourse.bacc as bacc
    from concourse.bass_utils import run_bass_kernel_spmd

    x = np.ascontiguousarray(inputs["x"])
    batch, seq, width = x.shape
    x = x.reshape(batch * seq, width)
    arrays = {
        "x": x,
        "x_t": np.ascontiguousarray(x.T),
        "cat": np.ascontiguousarray(inputs["itok_B_0_63"]).reshape(1, batch),
        "cond_w": np.ascontiguousarray(inputs["L0_cond_W"]),
        "cond_wt": np.ascontiguousarray(np.transpose(inputs["L0_cond_W"], (0, 2, 1))),
        "cond_b": np.ascontiguousarray(inputs["L0_cond_b"]),
        "w_r": np.ascontiguousarray(inputs["L0_ffn_Wr"]),
        "w_1": np.ascontiguousarray(inputs["L0_ffn_W1"]),
        "w_2": np.ascontiguousarray(inputs["L0_ffn_W2"]),
    }
    nc = bacc.Bacc("TRN2", target_bir_lowering=False, num_devices=1)
    args = [nc.dram_tensor(n, a.shape, mybir.dt.from_np(a.dtype), kind="ExternalInput").ap()
            for n, a in arrays.items()]
    out = nc.dram_tensor("out", x.shape, mybir.dt.float32, kind="ExternalOutput").ap()
    h_rows = nc.dram_tensor("h_rows", x.shape, mybir.dt.float32).ap()
    moe_kernel(nc, *args, out, h_rows)
    r = run_bass_kernel_spmd(nc, [arrays], core_ids=[0])
    return r.results[0]["out"].reshape(batch, seq, width)
```
